# Optimizing a Trainium2 kernel written in Bass

```python
import numpy as np
import jax
import jax.numpy as jnp

def _softmax(x, axis=-1):
    return jax.nn.softmax(x, axis=axis)
def _gelu(x):
    return jax.nn.gelu(x, approximate=True)
def _silu(x):
    return jax.nn.silu(x)
def _sigmoid(x):
    return jax.nn.sigmoid(x)
def _layernorm(x, axis=-1, eps=1e-5):
    m = jnp.mean(x, axis=axis, keepdims=True)
    v = jnp.var(x, axis=axis, keepdims=True)
    return (x - m) / jnp.sqrt(v + eps)
def _scatter_add(tgt, idx, src, axis=0):
    return tgt.at[idx].add(src)
def _segment_sum(src, seg, n):
    return jax.ops.segment_sum(src, seg, n)

kernel_name = 'mk_rec_standalone_d1_rec_f0367d'

def setup_inputs(seed: int = 0):
    np.random.seed(seed)
    _w = jnp.asarray
    def _rec_inputs():
        import jax
        import jax.numpy as jnp
        _rk = jax.random.key(seed)
        r_X = -7.10856e-05 + 0.999911 * jax.random.normal(jax.random.fold_in(_rk, 1), (16384, 4096), jnp.float32)
        return r_X
    r_X = _rec_inputs()
    def _L0_rec_setup():
        import jax, jax.numpy as jnp
        import numpy as np
        B = 16384
        D = 4096
        key = jax.random.key(seed)
        kx, ka = jax.random.split(key)
        X = jax.random.normal(kx, (B, D), dtype=jnp.float32)
        stdv = 1.0 / np.sqrt(D)
        alphas = jax.random.uniform(ka, (D,), dtype=jnp.float32, minval=-stdv, maxval=stdv)
        bias = jnp.zeros((D,), dtype=jnp.float32)
        return {'X': X, 'alphas': alphas, 'bias': bias}
    _L0_rec_all = _L0_rec_setup()
    _L0_rec_in = {k: v for k, v in _L0_rec_all.items() if k in ('alphas', 'bias', )}
    del _L0_rec_all

    return {
        "r_X": r_X,
        "L0_rec_alphas": _L0_rec_in["alphas"],
        "L0_rec_bias": _L0_rec_in["bias"],
    }

def reference(r_X, L0_rec_alphas, L0_rec_bias):
    import jax
    import jax.numpy as jnp
    def _L0_rec_ref(X, alphas, bias):
        import jax, jax.numpy as jnp
        import numpy as np
        B = 16384
        D = 4096
        xa = X @ alphas
        val = X * xa[:, None]
        return val + bias + X

    y = _L0_rec_ref(r_X, L0_rec_alphas, L0_rec_bias)
    return y


_drawn_inputs = setup_inputs


def setup_inputs(seed=0):
    import zlib

    import numpy as np

    out = dict(_drawn_inputs(seed))
    spreads = {'L0_rec_bias': (0.0, 0.1)}
    factors = {}
    for name, (base, spread) in spreads.items():
        noise = np.random.default_rng([zlib.crc32(name.encode()), seed]).standard_normal(out[name].shape)
        drawn = base * np.exp(spread * noise) if base else spread * noise
        out[name] = jnp.asarray(drawn.astype(out[name].dtype))
    for name, factor in factors.items():
        out[name] = (out[name] * factor).astype(out[name].dtype)
    return out
```

```python
import concourse.bass as bass
from concourse import mybir
from contextlib import ExitStack


def rec_kernel(nc: bass.Bass, X: bass.AP, alphas: bass.AP, bias: bass.AP, out: bass.AP):
    fp32 = mybir.dt.float32
    ALU = mybir.AluOpType
    ACT = mybir.ActivationFunctionType

    P = 128
    ROWS, D = X.shape
    TILES = ROWS // P
    SLOTS = 8
    ROUNDS = TILES // SLOTS
    BANK = 512
    BANKS = D // BANK

    x_tiles = X.rearrange("(t p) d -> t p d", p=P)
    out_tiles = out.rearrange("(t p) d -> t p d", p=P)
    alphas_dram = alphas.rearrange("(o d) -> o d", o=1)
    bias_dram = bias.rearrange("(o d) -> o d", o=1)

    with ExitStack() as ctx:
        def sb(name, shape):
            return ctx.enter_context(nc.sbuf_tensor(name, shape, fp32))

        def sem(name):
            return ctx.enter_context(nc.semaphore(name))

        x = [sb(f"x{s}", [P, D]) for s in range(SLOTS)]
        alphas_all = sb("alphas_all", [P, D])
        products = sb("products", [P, D])
        alphas_row = sb("alphas_row", [1, D])
        bias_row = sb("bias_row", [1, D])
        ones = sb("ones", [1, P])
        dot = sb("dot", [P, SLOTS])
        gain = sb("gain", [P, SLOTS])
        bias_all = ctx.enter_context(nc.psum_tensor("bias_all", [P, D], fp32))

        row_loaded = [sem("alphas_row_loaded"), sem("bias_row_loaded")]
        ones_set = sem("ones_set")
        alphas_spread = sem("alphas_spread")
        alphas_copied = sem("alphas_copied")
        bias_spread = sem("bias_spread")
        x_loaded = [sem(f"x{s}_loaded") for s in range(SLOTS)]
        x_stored = [sem(f"x{s}_stored") for s in range(SLOTS)]
        dot_done = sem("dot_done")
        gain_ready = sem("gain_ready")
        scaled = sem("scaled")

        block = ctx.enter_context(nc.Block())

        @block.sync
        def _(sp):
            def load(tile, s):
                sp.dma_start(x[s][:], x_tiles[tile]).then_inc(x_loaded[s], 16)

            sp.dma_start(alphas_row[:], alphas_dram).then_inc(row_loaded[0], 16)
            for s in range(SLOTS):
                load(s, s)
            with sp.Fori(1, ROUNDS) as r:
                for s in range(SLOTS):
                    sp.wait_ge(x_stored[s], r * 16)
                    load(r * SLOTS + s, s)

        @block.tensor
        def _(pe):
            pe.wait_ge(ones_set, 1)
            pe.wait_ge(row_loaded[0], 16)
            for b in range(BANKS):
                c = slice(b * BANK, (b + 1) * BANK)
                nc.tensor.matmul(bias_all[:, c], ones[:], alphas_row[:, c],
                                 start=True, stop=True).then_inc(alphas_spread, 1)
            pe.wait_ge(row_loaded[1], 16)
            for b in range(BANKS):
                c = slice(b * BANK, (b + 1) * BANK)
                pe.wait_ge(alphas_copied, b + 1)
                nc.tensor.matmul(bias_all[:, c], ones[:], bias_row[:, c],
                                 start=True, stop=True).then_inc(bias_spread, 1)

        @block.vector
        def _(dve):
            def take_dot(s, before):
                if before is not None:
                    dve.wait_ge(dot_done, before)
                nc.vector.scalar_tensor_tensor(products[:], x[s][:], 1.0, alphas_all[:], ALU.mult, ALU.mult,
                                               accum_out=dot[:, s:s + 1]).then_inc(dot_done, 1)

            def scale(s):
                nc.vector.scalar_tensor_tensor(x[s][:], x[s][:], gain[:, s:s + 1], bias_all[:], ALU.mult, ALU.add
                                               ).then_inc(scaled, 1)

            nc.vector.memset(ones[:], 1.0).then_inc(ones_set, 1)
            dve.wait_ge(alphas_copied, BANKS)
            dve.wait_ge(x_loaded[0], 16)
            take_dot(0, None)
            dve.wait_ge(bias_spread, BANKS)
            with dve.Fori(0, ROUNDS - 1) as r:
                for s in range(SLOTS):
                    n = (s + 1) % SLOTS
                    dve.wait_ge(x_loaded[n], r * 16 + 16 * (1 + (s + 1) // SLOTS))
                    take_dot(n, r * SLOTS + s + 1)
                    dve.wait_ge(gain_ready, r * SLOTS + s + 1)
                    scale(s)
            for s in range(SLOTS):
                if s + 1 < SLOTS:
                    dve.wait_ge(x_loaded[s + 1], ROUNDS * 16)
                    take_dot(s + 1, (ROUNDS - 1) * SLOTS + s + 1)
                dve.wait_ge(gain_ready, (ROUNDS - 1) * SLOTS + s + 1)
                scale(s)

        @block.scalar
        def _(act):
            def add_one(s):
                nc.scalar.activation(gain[:, s:s + 1], dot[:, s:s + 1], ACT.Copy, bias=1.0).then_inc(gain_ready, 1)

            def store(tile, s):
                act.dma_start(out_tiles[tile], x[s][:]).then_inc(x_stored[s], 16)

            act.dma_start(bias_row[:], bias_dram).then_inc(row_loaded[1], 16)
            for b in range(BANKS):
                c = slice(b * BANK, (b + 1) * BANK)
                act.wait_ge(alphas_spread, b + 1)
                nc.scalar.copy(alphas_all[:, c], bias_all[:, c]).then_inc(alphas_copied, 1)
            act.wait_ge(dot_done, 1)
            add_one(0)
            with act.Fori(0, ROUNDS - 1) as r:
                for s in range(SLOTS):
                    act.wait_ge(dot_done, r * SLOTS + s + 2)
                    add_one((s + 1) % SLOTS)
                    act.wait_ge(scaled, r * SLOTS + s + 1)
                    store(r * SLOTS + s, s)
            for s in range(SLOTS):
                tile = (ROUNDS - 1) * SLOTS + s
                if s + 1 < SLOTS:
                    act.wait_ge(dot_done, tile + 2)
                    add_one(s + 1)
                act.wait_ge(scaled, tile + 1)
                store(tile, s)
            for s in range(SLOTS):
                act.wait_ge(x_stored[s], ROUNDS * 16)


def kernel(**inputs):
    import numpy as _np
    import concourse.bacc as _bacc
    from concourse import mybir as _mybir
    from concourse.bass_utils import run_bass_kernel_spmd as _run

    nc = _bacc.Bacc("TRN2", target_bir_lowering=False, num_devices=1)
    arrays, args = {}, []
    for name in ("r_X", "L0_rec_alphas", "L0_rec_bias"):
        a = _np.ascontiguousarray(inputs[name])
        arrays[f"in_{name}"] = a
        args.append(nc.dram_tensor(f"in_{name}", a.shape, _mybir.dt.from_np(a.dtype), kind="ExternalInput").ap())
    x = arrays["in_r_X"]
    args.append(nc.dram_tensor("out_y", x.shape, _mybir.dt.from_np(x.dtype), kind="ExternalOutput").ap())
    rec_kernel(nc, *args)
    r = _run(nc, [arrays], core_ids=[0])
    return r.results[0]["out_y"]
```
